# Optimizing a Trainium2 kernel written in Bass

```python
import numpy as np
import jax
import jax.numpy as jnp

def _softmax(x, axis=-1):
    return jax.nn.softmax(x, axis=axis)

def _gelu(x):
    return jax.nn.gelu(x, approximate=True)

def _silu(x):
    return jax.nn.silu(x)

def _sigmoid(x):
    return jax.nn.sigmoid(x)

def _layernorm(x, axis=-1, eps=1e-05):
    m = jnp.mean(x, axis=axis, keepdims=True)
    v = jnp.var(x, axis=axis, keepdims=True)
    return (x - m) / jnp.sqrt(v + eps)

def _scatter_add(tgt, idx, src, axis=0):
    return tgt.at[idx].add(src)

def _segment_sum(src, seg, n):
    return jax.ops.segment_sum(src, seg, n)
kernel_name = 'mk_rec_standalone_d1_rec_r8_38f9f7'

def setup_inputs(seed: int=0):
    np.random.seed(seed)
    _w = jnp.asarray

    def _rec_inputs():
        import jax
        import jax.numpy as jnp
        _rk = jax.random.key(seed)
        r_state = -0.000928989 + 1.00043 * jax.random.normal(jax.random.fold_in(_rk, 1), (512, 256), jnp.float32)
        r_token = jax.random.randint(jax.random.fold_in(_rk, 2), (512,), 49, 31986, jnp.int32)
        return (r_state, r_token)
    r_state, r_token = _rec_inputs()

    def _L0_rec_setup():
        import jax, jax.numpy as jnp
        import numpy as np
        VOCAB = 4000
        HIDDEN = 256
        NLAYERS = 6
        BATCH = 512
        key = jax.random.key(seed)
        k1, k2, k3, k4 = jax.random.split(key, 4)
        state = jax.random.normal(k1, (BATCH, HIDDEN), dtype=jnp.float32)
        token = jax.random.randint(k2, (BATCH,), 0, VOCAB, dtype=jnp.int32)
        ih = jax.random.normal(k3, (NLAYERS, VOCAB, HIDDEN), dtype=jnp.float32) * 0.02
        hh = jax.random.normal(k4, (NLAYERS, HIDDEN, HIDDEN), dtype=jnp.float32) * 0.02
        return {'state': state, 'token': token, 'ih': ih, 'hh': hh}
    _L0_rec_all = _L0_rec_setup()
    _L0_rec_in = {k: v for k, v in _L0_rec_all.items() if k in ('ih', 'hh')}
    del _L0_rec_all
    return {'r_state': r_state, 'r_token': r_token, 'L0_rec_ih': _L0_rec_in['ih'], 'L0_rec_hh': _L0_rec_in['hh']}

def reference(r_state, r_token, L0_rec_ih, L0_rec_hh):
    import jax
    import jax.numpy as jnp

    def _L0_rec_ref(state, token, ih, hh):
        import jax, jax.numpy as jnp
        import numpy as np
        VOCAB = 4000
        HIDDEN = 256
        NLAYERS = 6
        BATCH = 512
        n_layers = ih.shape[0]
        for i in range(n_layers):
            gate = ih[i][token]
            state = jnp.tanh(state + jnp.matmul(state, hh[i]) * gate)
        return state
    y = _L0_rec_ref(r_state, r_token, L0_rec_ih, L0_rec_hh)
    return y

_drawn_inputs = setup_inputs


def setup_inputs(seed=0):
    import zlib

    import numpy as np

    out = dict(_drawn_inputs(seed))
    spreads = {}
    factors = {'L0_rec_ih': 3.856, 'L0_rec_hh': 3.837}
    for name, (base, spread) in spreads.items():
        noise = np.random.default_rng([zlib.crc32(name.encode()), seed]).standard_normal(out[name].shape)
        drawn = base * np.exp(spread * noise) if base else spread * noise
        out[name] = jnp.asarray(drawn.astype(out[name].dtype))
    for name, factor in factors.items():
        out[name] = (out[name] * factor).astype(out[name].dtype)
    return out
```

```python
import concourse.bass as bass
from concourse import mybir
from contextlib import ExitStack


def gated_recurrence(nc, r_state, r_token, ih, hh, out):
    fp32, i32 = mybir.dt.float32, mybir.dt.int32
    ALU = mybir.AluOpType
    ACT = mybir.ActivationFunctionType

    BATCH, HIDDEN = r_state.shape
    LAYERS, VOCAB, _ = ih.shape
    P = 128
    TILES = BATCH // P
    KC = HIDDEN // P
    STEPS = LAYERS * TILES
    LAG = 2

    state_rows = r_state.rearrange("(p t) h -> p (t h)", t=TILES)
    out_rows = out.rearrange("(p t) h -> p t h", t=TILES)
    token_rows = r_token.rearrange("(p t) -> p t", t=TILES)
    ih_rows = ih.rearrange("l v h -> (l v) h")
    hh_rows = hh.rearrange("l (k p) h -> p l k h", p=P)

    ctx = ExitStack()
    with ctx:
        def sb(name, shape, dt=fp32):
            return ctx.enter_context(nc.sbuf_tensor(name, shape, dt))

        def sem(name):
            return ctx.enter_context(nc.semaphore(name))

        state = sb("state", [P, TILES, HIDDEN])
        state_t = sb("state_t", [P, TILES, KC, P])
        pre = sb("pre", [P, TILES, HIDDEN])
        weights = sb("weights", [P, LAYERS, KC, HIDDEN])
        gates = sb("gates", [P, LAYERS, TILES, HIDDEN])
        token = sb("token", [P, TILES], i32)
        wrap = sb("wrap", [P, TILES], i32)
        wrapped = sb("wrapped", [P, TILES], i32)
        row = sb("row", [P, TILES], i32)
        ident = sb("ident", [P, P])
        product = [ctx.enter_context(nc.psum_tensor(f"product{t}", [P, 512], fp32)) for t in range(TILES)]
        turned = [ctx.enter_context(nc.psum_tensor(f"turned{t}", [P, 512], fp32)) for t in range(TILES)]

        token_in = sem("token_in")
        state_in = sem("state_in")
        weights_in = [sem(f"weights_in{l}") for l in range(LAYERS)]
        gates_in = [sem(f"gates_in{l}") for l in range(LAYERS)]
        row_step = sem("row_step")
        ident_ready = sem("ident_ready")
        turned_ready = sem("turned_ready")
        state_t_ready = sem("state_t_ready")
        product_ready = sem("product_ready")
        gated = sem("gated")
        pre_ready = sem("pre_ready")
        state_ready = sem("state_ready")
        out_done = sem("out_done")

        block = ctx.enter_context(nc.Block())

        @block.sync
        def _(sp):
            sp.dma_start(token[:, :], token_rows).then_inc(token_in, 16)
            sp.dma_start(state[:, :, :].rearrange("p t h -> p (t h)"), state_rows).then_inc(state_in, 16)
            for l in range(LAYERS):
                sp.dma_start(weights[:, l], hh_rows[:, l]).then_inc(weights_in[l], 16)
            for t in range(TILES):
                sp.wait_ge(state_ready, STEPS - TILES + t + 1)
                sp.dma_start(out_rows[:, t], state[:, t]).then_inc(out_done, 16)
            sp.wait_ge(out_done, 16 * TILES)

        @block.gpsimd
        def _(pool):
            nc.gpsimd.memset(ident[:], 0.0).then_inc(ident_ready, 1)
            pool.wait_ge(ident_ready, 1)
            nc.gpsimd.affine_select(out=ident[:], in_=ident[:], compare_op=ALU.not_equal, fill=1.0, base=0,
                                    pattern=[[-1, P]], channel_multiplier=1).then_inc(ident_ready, 1)
            pool.wait_ge(row_step, 3)
            for l in range(LAYERS):
                for t in range(TILES):
                    nc.gpsimd.indirect_dma_start(
                        out=gates[:, l, t], out_offset=None, in_=ih_rows,
                        in_offset=bass.IndirectOffsetOnAxis(ap=row[:, t:t + 1], axis=0),
                        element_offset=l * VOCAB * HIDDEN).then_inc(gates_in[l], 16)

        @block.vector
        def _(dve):
            dve.wait_ge(token_in, 16)
            nc.vector.tensor_scalar(wrap[:], token[:], 0, VOCAB, ALU.is_lt, ALU.mult).then_inc(row_step, 1)
            dve.wait_ge(row_step, 1)
            nc.vector.scalar_tensor_tensor(out=wrapped[:], in0=token[:], scalar=VOCAB - 1, in1=wrap[:],
                                           op0=ALU.min, op1=ALU.add).then_inc(row_step, 1)
            dve.wait_ge(row_step, 2)
            nc.vector.tensor_scalar(row[:], wrapped[:], 0, None, ALU.max).then_inc(row_step, 1)
            for n in range(STEPS):
                l, t = divmod(n, TILES)
                if t == 0:
                    dve.wait_ge(gates_in[l], 16 * TILES)
                dve.wait_ge(product_ready, n + 1)
                nc.vector.tensor_tensor(product[t][:, 0:HIDDEN], product[t][:, 0:HIDDEN], gates[:, l, t],
                                        ALU.mult).then_inc(gated, 1)
                dve.wait_ge(gated, n + 1)
                if n == 0:
                    dve.wait_ge(state_in, 16)
                nc.vector.tensor_tensor(pre[:, t], product[t][:, 0:HIDDEN], state[:, t],
                                        ALU.add).then_inc(pre_ready, 1)

        @block.scalar
        def _(act):
            def to_sbuf(n):
                act.wait_ge(turned_ready, n + 1)
                nc.scalar.activation(state_t[:, n % TILES].rearrange("p k c -> p (k c)"),
                                     turned[n % TILES][:, 0:HIDDEN], ACT.Copy).then_inc(state_t_ready, 1)

            for t in range(TILES):
                to_sbuf(t)
            for n in range(STEPS):
                l, t = divmod(n, TILES)
                act.wait_ge(pre_ready, n + 1)
                nc.scalar.activation(state[:, t], pre[:, t], ACT.Tanh).then_inc(state_ready, 1)
                if n >= LAG - 1 and n - LAG + 1 + TILES < STEPS:
                    to_sbuf(n - LAG + 1 + TILES)

        @block.tensor
        def _(pe):
            def turn(n):
                t = n % TILES
                if n >= TILES:
                    pe.wait_ge(state_ready, n - TILES + 1)
                for k in range(KC):
                    last = nc.tensor.matmul(turned[t][:, k * P:(k + 1) * P], state[:, t, k * P:(k + 1) * P],
                                            ident[:], is_transpose=True, start=(k == 0), stop=(k == KC - 1),
                                            skip_group_check=True)
                last.then_inc(turned_ready, 1)

            pe.wait_ge(ident_ready, 2)
            pe.wait_ge(state_in, 16)
            for t in range(TILES):
                turn(t)
            for n in range(STEPS):
                l, t = divmod(n, TILES)
                if t == 0:
                    pe.wait_ge(weights_in[l], 16)
                pe.wait_ge(state_t_ready, n + 1)
                if n >= TILES:
                    pe.wait_ge(pre_ready, n - TILES + 1)
                for k in range(KC):
                    last = nc.tensor.matmul(product[t][:, 0:HIDDEN], state_t[:, t, k], weights[:, l, k],
                                            start=(k == 0), stop=(k == KC - 1))
                last.then_inc(product_ready, 1)
                if n >= LAG and n - LAG + TILES < STEPS:
                    turn(n - LAG + TILES)


_INS = ["r_state", "r_token", "L0_rec_ih", "L0_rec_hh"]


def kernel(**inputs):
    import numpy as _np
    import concourse.bacc as _bacc
    from concourse import mybir as _mybir
    from concourse.bass_utils import run_bass_kernel_spmd as _run

    nc = _bacc.Bacc("TRN2", target_bir_lowering=False, num_devices=1)
    arrays, args = {}, []
    for name in _INS:
        a = _np.ascontiguousarray(inputs[name])
        arrays[f"in_{name}_dram"] = a
        args.append(nc.dram_tensor(f"in_{name}_dram", a.shape, _mybir.dt.from_np(a.dtype), kind="ExternalInput").ap())
    shape = inputs["r_state"].shape
    args.append(nc.dram_tensor("out_dram", shape, _mybir.dt.float32, kind="ExternalOutput").ap())
    gated_recurrence(nc, *args)
    r = _run(nc, [arrays], core_ids=[0])
    return r.results[0]["out_dram"]
```

```python
import concourse.bass as bass
from concourse import mybir
from contextlib import ExitStack


def gated_recurrence(nc, state_rows, state_cols, tokens, table, matrices, out):
    fp32, i32, bf16 = mybir.dt.float32, mybir.dt.int32, mybir.dt.bfloat16
    ALU = mybir.AluOpType
    ACT = mybir.ActivationFunctionType

    P, TILES, HIDDEN = state_rows.shape
    VOCAB, LAYERS, _ = table.shape
    KC = HIDDEN // P
    STEPS = LAYERS * TILES
    LAG = 2
    WARM_UPS = 7
    SPANS = [(0, 1), (1, 3), (3, LAYERS)]

    table_rows = table.rearrange("v l h -> v (l h)")
    span_of = [next(i for i, (a, b) in enumerate(SPANS) if a <= l < b) for l in range(LAYERS)]

    ctx = ExitStack()
    with ctx:
        def sb(name, shape, dt=fp32):
            return ctx.enter_context(nc.sbuf_tensor(name, shape, dt))

        def sem(name):
            return ctx.enter_context(nc.semaphore(name))

        state = sb("state", [P, TILES, HIDDEN])
        state_t = sb("state_t", [P, TILES, KC, P])
        pre = sb("pre", [P, TILES, HIDDEN])
        weights = sb("weights", [P, LAYERS, KC, HIDDEN])
        gates = sb("gates", [P, TILES, LAYERS, HIDDEN])
        token = sb("token", [P, TILES], i32)
        wrap = sb("wrap", [P, TILES], i32)
        clipped = sb("clipped", [P, TILES], i32)
        row = sb("row", [P, TILES], i32)
        ident = sb("ident", [P, P])
        zeros = sb("zeros", [P, 512], bf16)
        product = [ctx.enter_context(nc.psum_tensor(f"product{t}", [P, 512], fp32)) for t in range(TILES)]
        turned = [ctx.enter_context(nc.psum_tensor(f"turned{t}", [P, 512], fp32)) for t in range(TILES)]

        token_in = sem("token_in")
        state_in = sem("state_in")
        first_col_in = sem("first_col_in")
        cols_in = sem("cols_in")
        weights_in = [sem(f"weights_in{l}") for l in range(LAYERS)]
        gates_in = [[sem(f"gates_in{t}_{s}") for s in range(len(SPANS))] for t in range(TILES)]
        zeros_ready = sem("zeros_ready")
        row_step = sem("row_step")
        ident_ready = sem("ident_ready")
        turned_ready = sem("turned_ready")
        state_t_ready = sem("state_t_ready")
        product_ready = sem("product_ready")
        gated = sem("gated")
        pre_ready = sem("pre_ready")
        state_ready = sem("state_ready")
        out_done = sem("out_done")

        block = ctx.enter_context(nc.Block())

        @block.sync
        def _(sp):
            sp.dma_start(token[:, :], tokens).then_inc(token_in, 16)
            sp.dma_start(weights[:, 0], matrices[:, 0]).then_inc(weights_in[0], 16)
            sp.dma_start(state_t[:, 0], state_cols[:, 0]).then_inc(first_col_in, 16)
            sp.dma_start(state_t[:, 1:TILES], state_cols[:, 1:TILES]).then_inc(cols_in, 16)
            sp.dma_start(state[:, :, :], state_rows).then_inc(state_in, 16)
            for l in range(1, LAYERS):
                sp.wait_ge(product_ready, (l - 1) * TILES // 2 + 1)
                sp.dma_start(weights[:, l], matrices[:, l]).then_inc(weights_in[l], 16)
            for t in range(TILES):
                sp.wait_ge(state_ready, STEPS - TILES + t + 1)
                sp.dma_start(out[:, t], state[:, t]).then_inc(out_done, 16)
            sp.wait_ge(out_done, 16 * TILES)

        @block.gpsimd
        def _(pool):
            nc.gpsimd.memset(ident[:], 0.0).then_inc(ident_ready, 1)
            pool.wait_ge(ident_ready, 1)
            nc.gpsimd.affine_select(out=ident[:], in_=ident[:], compare_op=ALU.not_equal, fill=1.0, base=0,
                                    pattern=[[-1, P]], channel_multiplier=1).then_inc(ident_ready, 1)
            pool.wait_ge(row_step, 3)
            for s, (a, b) in enumerate(SPANS):
                for t in range(TILES):
                    nc.gpsimd.indirect_dma_start(
                        out=gates[:, t, a:b].rearrange("p l h -> p (l h)"), out_offset=None, in_=table_rows,
                        in_offset=bass.IndirectOffsetOnAxis(ap=row[:, t:t + 1], axis=0),
                        element_offset=a * HIDDEN).then_inc(gates_in[t][s], 16)

        @block.vector
        def _(dve):
            nc.vector.memset(zeros[:], 0.0).then_inc(zeros_ready, 1)
            dve.wait_ge(token_in, 16)
            nc.vector.tensor_scalar(wrap[:], token[:], 0, VOCAB, ALU.is_lt, ALU.mult).then_inc(row_step, 1)
            nc.vector.tensor_scalar(clipped[:], token[:], -VOCAB, VOCAB - 1, ALU.max, ALU.min).then_inc(row_step, 1)
            dve.wait_ge(row_step, 2)
            nc.vector.tensor_tensor(row[:], clipped[:], wrap[:], ALU.add).then_inc(row_step, 1)
            for n in range(STEPS):
                l, t = divmod(n, TILES)
                if l == SPANS[span_of[l]][0]:
                    dve.wait_ge(gates_in[t][span_of[l]], 16)
                dve.wait_ge(product_ready, n + 1)
                nc.vector.tensor_tensor(product[t][:, 0:HIDDEN], product[t][:, 0:HIDDEN], gates[:, t, l],
                                        ALU.mult).then_inc(gated, 1)
                dve.wait_ge(gated, n + 1)
                if n == 0:
                    dve.wait_ge(state_in, 16)
                nc.vector.tensor_tensor(pre[:, t], product[t][:, 0:HIDDEN], state[:, t],
                                        ALU.add).then_inc(pre_ready, 1)

        @block.scalar
        def _(act):
            for n in range(STEPS):
                t = n % TILES
                act.wait_ge(pre_ready, n + 1)
                nc.scalar.activation(state[:, t], pre[:, t], ACT.Tanh).then_inc(state_ready, 1)
                m = n - LAG + 1
                if 0 <= m < STEPS - TILES:
                    act.wait_ge(turned_ready, m + 1)
                    nc.scalar.activation(state_t[:, m % TILES].rearrange("p k c -> p (k c)"),
                                         turned[m % TILES][:, 0:HIDDEN], ACT.Copy).then_inc(state_t_ready, 1)

        @block.tensor
        def _(pe):
            def turn(n):
                t = n % TILES
                pe.wait_ge(state_ready, n + 1)
                if n >= TILES:
                    pe.wait_ge(state_t_ready, n - TILES + 1)
                for k in range(KC):
                    last = nc.tensor.matmul(turned[t][:, k * P:(k + 1) * P], state[:, t, k * P:(k + 1) * P],
                                            ident[:], is_transpose=True, start=(k == 0), stop=(k == KC - 1),
                                            skip_group_check=True)
                last.then_inc(turned_ready, 1)

            pe.wait_ge(zeros_ready, 1)
            for _ in range(WARM_UPS):
                nc.tensor.matmul(product[0][:, :], zeros[:, 0:P], zeros[:, :], start=True, stop=True)
            for n in range(STEPS):
                l, t = divmod(n, TILES)
                if t == 0:
                    pe.wait_ge(weights_in[l], 16)
                if n < 2:
                    pe.wait_ge(first_col_in if n == 0 else cols_in, 16)
                if n >= TILES:
                    pe.wait_ge(state_t_ready, n - TILES + 1)
                    pe.wait_ge(pre_ready, n - TILES + 1)
                for k in range(KC):
                    last = nc.tensor.matmul(product[t][:, 0:HIDDEN], state_t[:, t, k], weights[:, l, k],
                                            start=(k == 0), stop=(k == KC - 1))
                last.then_inc(product_ready, 1)
                if n == LAG:
                    pe.wait_ge(ident_ready, 2)
                if LAG <= n < STEPS - TILES + LAG:
                    turn(n - LAG)


def kernel(**inputs):
    import numpy as _np
    import concourse.bacc as _bacc
    from concourse import mybir as _mybir
    from concourse.bass_utils import run_bass_kernel_spmd as _run

    state, token, ih, hh = (_np.asarray(inputs[n]) for n in ("r_state", "r_token", "L0_rec_ih", "L0_rec_hh"))
    (batch, hidden), layers, p = state.shape, hh.shape[0], 128
    rows = state.reshape(p, batch // p, hidden)
    laid = {
        "state_rows": rows,
        "state_cols": rows.reshape(p, batch // p, hidden // p, p).transpose(3, 1, 2, 0),
        "tokens": token.reshape(p, batch // p),
        "table": ih.transpose(1, 0, 2),
        "matrices": hh.reshape(layers, hidden // p, p, hidden).transpose(2, 0, 1, 3),
    }
    nc = _bacc.Bacc("TRN2", target_bir_lowering=False, num_devices=1)
    arrays = {f"in_{n}": _np.ascontiguousarray(a) for n, a in laid.items()}
    args = [nc.dram_tensor(n, a.shape, _mybir.dt.from_np(a.dtype), kind="ExternalInput").ap()
            for n, a in arrays.items()]
    args.append(nc.dram_tensor("out_dram", rows.shape, _mybir.dt.float32, kind="ExternalOutput").ap())
    gated_recurrence(nc, *args)
    r = _run(nc, [arrays], core_ids=[0])
    return r.results[0]["out_dram"].reshape(batch, hidden)
```

```python
import concourse.bass as bass
from concourse import mybir
from contextlib import ExitStack


def gated_recurrence(nc, state_rows, state_cols, tokens, table, matrices, out):
    fp32, fp32r, i32, bf16 = mybir.dt.float32, mybir.dt.float32r, mybir.dt.int32, mybir.dt.bfloat16
    ALU = mybir.AluOpType
    ACT = mybir.ActivationFunctionType

    P, TILES, HIDDEN = state_rows.shape
    VOCAB, LAYERS, _ = table.shape
    KC = HIDDEN // P
    STEPS = LAYERS * TILES
    TURNS = STEPS - TILES
    LAG = 2
    WARM_UPS = 8
    SPANS = [(0, 1), (1, 3), (3, LAYERS)]
    FIRST_SPLIT = 1

    def is_split(n):
        return n >= FIRST_SPLIT * TILES and n % TILES in (0, 2)

    def rests(n):
        return sum(is_split(m + TILES) for m in range(n + 1))

    def gates_from(l):
        return next((s for s, (a, _) in enumerate(SPANS) if a == l), None)

    table_rows = table.rearrange("v l h -> v (l h)")

    ctx = ExitStack()
    with ctx:
        def sb(name, shape, dt=fp32):
            return ctx.enter_context(nc.sbuf_tensor(name, shape, dt))

        def sem(name):
            return ctx.enter_context(nc.semaphore(name))

        state = sb("state", [P, TILES, HIDDEN])
        first_cols = sb("first_cols", [P, TILES, KC * P])
        cols = sb("cols", [P, TILES, KC * P])
        cols_hi = sb("cols_hi", [P, TILES, KC * P], fp32r)
        cols_lo = sb("cols_lo", [P, TILES, KC * P], fp32r)
        pre = sb("pre", [P, TILES, HIDDEN])
        weights = sb("weights", [P, LAYERS, KC * HIDDEN])
        weights_hi = sb("weights_hi", [P, LAYERS, KC * HIDDEN], fp32r)
        weights_lo = sb("weights_lo", [P, LAYERS, KC * HIDDEN], fp32r)
        gates = sb("gates", [P, TILES, LAYERS, HIDDEN])
        token = sb("token", [P, TILES], i32)
        wrap = sb("wrap", [P, TILES], i32)
        clipped = sb("clipped", [P, TILES], i32)
        row = sb("row", [P, TILES], i32)
        ident = sb("ident", [P, P])
        zeros = sb("zeros", [P, 512], bf16)
        product = [ctx.enter_context(nc.psum_tensor(f"product{t}", [P, 512], fp32)) for t in range(TILES)]
        turned = [ctx.enter_context(nc.psum_tensor(f"turned{t}", [P, 512], fp32)) for t in range(TILES)]

        token_in = sem("token_in")
        state_in = [sem(f"state_in{i}") for i in range(3)]
        first_cols_in = sem("first_cols_in")
        cols_in = sem("cols_in")
        weights_in = [sem(f"weights_in{l}") for l in range(LAYERS)]
        gates_in = [[sem(f"gates_in{t}_{s}") for s in range(len(SPANS))] for t in range(TILES)]
        zeros_ready = sem("zeros_ready")
        ident_ready = sem("ident_ready")
        row_step = sem("row_step")
        first_lo_ready = sem("first_lo_ready")
        weights_hi_ready = sem("weights_hi_ready")
        weights_lo_ready = sem("weights_lo_ready")
        product_ready = sem("product_ready")
        gated = sem("gated")
        pre_ready = sem("pre_ready")
        state_ready = sem("state_ready")
        turned_ready = sem("turned_ready")
        cols_ready = sem("cols_ready")
        rest_ready = sem("rest_ready")
        out_done = sem("out_done")

        block = ctx.enter_context(nc.Block())

        @block.sync
        def _(sp):
            def load_weights(l):
                sp.dma_start(weights[:, l], matrices[:, l]).then_inc(weights_in[l], 16)

            sp.dma_start(token[:, :], tokens).then_inc(token_in, 16)
            load_weights(0)
            sp.dma_start(first_cols[:, 0], state_cols[:, 0]).then_inc(first_cols_in, 16)
            load_weights(1)
            sp.dma_start(first_cols[:, 1:TILES], state_cols[:, 1:TILES]).then_inc(cols_in, 16)
            sp.dma_start(state[:, 0], state_rows[:, 0]).then_inc(state_in[0], 16)
            sp.wait_ge(weights_in[1], 16)
            sp.dma_start(state[:, 1], state_rows[:, 1]).then_inc(state_in[1], 16)
            sp.dma_start(state[:, 2:TILES], state_rows[:, 2:TILES]).then_inc(state_in[2], 16)
            for l in range(2, LAYERS):
                sp.wait_ge(product_ready, (l - 2) * TILES + 1)
                load_weights(l)
            for t in range(TILES):
                sp.wait_ge(state_ready, TURNS + t + 1)
                sp.dma_start(out[:, t], state[:, t]).then_inc(out_done, 16)
            sp.wait_ge(out_done, 16 * TILES)

        @block.gpsimd
        def _(pool):
            def gather(s, t):
                a, b = SPANS[s]
                nc.gpsimd.indirect_dma_start(
                    out=gates[:, t, a:b].rearrange("p l h -> p (l h)"), out_offset=None, in_=table_rows,
                    in_offset=bass.IndirectOffsetOnAxis(ap=row[:, t:t + 1], axis=0),
                    element_offset=a * HIDDEN).then_inc(gates_in[t][s], 16)

            def split_weights(l):
                pool.wait_ge(weights_hi_ready, l)
                nc.gpsimd.tensor_tensor(weights_lo[:, l], weights[:, l], weights_hi[:, l].bitcast(fp32),
                                        ALU.subtract).then_inc(weights_lo_ready, 1)

            nc.gpsimd.memset(ident[:], 0.0).then_inc(ident_ready, 1)
            pool.wait_ge(ident_ready, 1)
            nc.gpsimd.affine_select(out=ident[:], in_=ident[:], compare_op=ALU.not_equal, fill=1.0, base=0,
                                    pattern=[[-1, P]], channel_multiplier=1).then_inc(ident_ready, 1)
            pool.wait_ge(row_step, 3)
            for s in range(2):
                for t in range(TILES):
                    gather(s, t)
            split_weights(2)
            gather(2, 0)
            gather(2, 1)
            split_weights(3)
            gather(2, 2)
            gather(2, 3)
            split_weights(4)
            split_weights(5)

        @block.vector
        def _(dve):
            nc.vector.memset(zeros[:], 0.0).then_inc(zeros_ready, 1)
            dve.wait_ge(token_in, 16)
            nc.vector.tensor_scalar(wrap[:], token[:], 0, VOCAB, ALU.is_lt, ALU.mult).then_inc(row_step, 1)
            nc.vector.tensor_scalar(clipped[:], token[:], -VOCAB, VOCAB - 1, ALU.max, ALU.min).then_inc(row_step, 1)
            dve.wait_ge(row_step, 2)
            nc.vector.tensor_tensor(row[:], clipped[:], wrap[:], ALU.add).then_inc(row_step, 1)

            dve.wait_ge(weights_hi_ready, 1)
            nc.vector.tensor_tensor(weights_lo[:, 1], weights[:, 1], weights_hi[:, 1].bitcast(fp32),
                                    ALU.subtract).then_inc(first_lo_ready, 1)

            for n in range(STEPS):
                l, t = divmod(n, TILES)
                if gates_from(l) is not None:
                    dve.wait_ge(gates_in[t][gates_from(l)], 16)
                dve.wait_ge(product_ready, n + 1)
                nc.vector.tensor_tensor(product[t][:, 0:HIDDEN], product[t][:, 0:HIDDEN], gates[:, t, l],
                                        ALU.mult).then_inc(gated, 1)
                if n < 3:
                    dve.wait_ge(state_in[n], 16)
                dve.wait_ge(gated, n + 1)
                nc.vector.tensor_tensor(pre[:, t], product[t][:, 0:HIDDEN], state[:, t],
                                        ALU.add).then_inc(pre_ready, 1)
                m = n - LAG
                if 0 <= m < TURNS and is_split(m + TILES):
                    dve.wait_ge(cols_ready, m + 1)
                    nc.vector.tensor_tensor(cols_lo[:, m % TILES], turned[m % TILES][:, 0:HIDDEN],
                                            cols_hi[:, m % TILES].bitcast(fp32),
                                            ALU.subtract).then_inc(rest_ready, 1)

        @block.scalar
        def _(act):
            def split_weights(l):
                act.wait_ge(weights_in[l], 16)
                nc.scalar.activation(weights_hi[:, l], weights[:, l], ACT.Copy).then_inc(weights_hi_ready, 1)

            split_weights(1)
            for n in range(STEPS):
                l, t = divmod(n, TILES)
                act.wait_ge(pre_ready, n + 1)
                nc.scalar.activation(state[:, t], pre[:, t], ACT.Tanh).then_inc(state_ready, 1)
                m = n - LAG + 1
                if 0 <= m < TURNS:
                    act.wait_ge(turned_ready, m + 1)
                    to = cols_hi if is_split(m + TILES) else cols
                    nc.scalar.activation(to[:, m % TILES], turned[m % TILES][:, 0:HIDDEN],
                                         ACT.Copy).then_inc(cols_ready, 1)
                if t == 2 and l + 2 < LAYERS:
                    split_weights(l + 2)

        @block.tensor
        def _(pe):
            def multiply(n, terms):
                l, t = divmod(n, TILES)
                for i, (left, right, k) in enumerate(terms):
                    if left is cols_lo and k == 0:
                        pe.wait_ge(rest_ready, rests(n - TILES))
                    last = nc.tensor.matmul(product[t][:, 0:HIDDEN], left[:, t, k * P:(k + 1) * P],
                                            right[:, l, k * HIDDEN:(k + 1) * HIDDEN],
                                            start=(i == 0), stop=(i == len(terms) - 1))
                last.then_inc(product_ready, 1)

            def turn(n):
                t = n % TILES
                pe.wait_ge(state_ready, n + 1)
                for k in range(KC):
                    last = nc.tensor.matmul(turned[t][:, k * P:(k + 1) * P], state[:, t, k * P:(k + 1) * P],
                                            ident[:], is_transpose=True, start=(k == 0), stop=(k == KC - 1),
                                            skip_group_check=True)
                last.then_inc(turned_ready, 1)

            pe.wait_ge(zeros_ready, 1)
            for _ in range(WARM_UPS):
                nc.tensor.matmul(product[0][:, :], zeros[:, 0:P], zeros[:, :], start=True, stop=True)
            pe.wait_ge(weights_in[0], 16)
            for n in range(STEPS):
                l, t = divmod(n, TILES)
                if n < TILES:
                    if n < 2:
                        pe.wait_ge(first_cols_in if n == 0 else cols_in, 16)
                    multiply(n, [(first_cols, weights, k) for k in range(KC)])
                else:
                    pe.wait_ge(cols_ready, n - TILES + 1)
                    pe.wait_ge(pre_ready, n - TILES + 1)
                    if is_split(n):
                        if t == 0:
                            if l == 1:
                                pe.wait_ge(first_lo_ready, 1)
                            else:
                                pe.wait_ge(weights_lo_ready, l - 1)
                        multiply(n, [(cols_hi, w, k) for k in range(KC) for w in (weights_hi, weights_lo)]
                                 + [(cols_lo, weights_hi, k) for k in range(KC)])
                    else:
                        multiply(n, [(cols, weights, k) for k in range(KC)])
                if n == LAG:
                    pe.wait_ge(ident_ready, 2)
                if LAG <= n < TURNS + LAG:
                    turn(n - LAG)


def kernel(**inputs):
    import numpy as _np
    import concourse.bacc as _bacc
    from concourse import mybir as _mybir
    from concourse.bass_utils import run_bass_kernel_spmd as _run

    state, token, ih, hh = (_np.asarray(inputs[n]) for n in ("r_state", "r_token", "L0_rec_ih", "L0_rec_hh"))
    (batch, hidden), layers, p = state.shape, hh.shape[0], 128
    rows = state.reshape(p, batch // p, hidden)
    laid = {
        "state_rows": rows,
        "state_cols": rows.reshape(p, batch // p, hidden // p, p).transpose(3, 1, 2, 0).reshape(p, batch // p, hidden),
        "tokens": token.reshape(p, batch // p),
        "table": ih.transpose(1, 0, 2),
        "matrices": hh.reshape(layers, hidden // p, p, hidden).transpose(2, 0, 1, 3).reshape(p, layers, -1),
    }
    nc = _bacc.Bacc("TRN2", target_bir_lowering=False, num_devices=1)
    arrays = {f"in_{n}": _np.ascontiguousarray(a) for n, a in laid.items()}
    args = [nc.dram_tensor(n, a.shape, _mybir.dt.from_np(a.dtype), kind="ExternalInput").ap()
            for n, a in arrays.items()]
    args.append(nc.dram_tensor("out_dram", rows.shape, _mybir.dt.float32, kind="ExternalOutput").ap())
    gated_recurrence(nc, *args)
    r = _run(nc, [arrays], core_ids=[0])
    return r.results[0]["out_dram"].reshape(batch, hidden)
```
